# Optimizing a Trainium2 kernel written in Bass

```python
import numpy as np
import jax
import jax.numpy as jnp

def _softmax(x, axis=-1):
    return jax.nn.softmax(x, axis=axis)

def _gelu(x):
    return jax.nn.gelu(x, approximate=True)

def _silu(x):
    return jax.nn.silu(x)

def _sigmoid(x):
    return jax.nn.sigmoid(x)

def _layernorm(x, axis=-1, eps=1e-05):
    m = jnp.mean(x, axis=axis, keepdims=True)
    v = jnp.var(x, axis=axis, keepdims=True)
    return (x - m) / jnp.sqrt(v + eps)

def _scatter_add(tgt, idx, src, axis=0):
    return tgt.at[idx].add(src)

def _segment_sum(src, seg, n):
    return jax.ops.segment_sum(src, seg, n)
kernel_name = 'mk_seq_postln_d2_jaxref_r8_7d7fbb'

def setup_inputs(seed: int=0):
    np.random.seed(seed)
    _w = jnp.asarray

    def _L0_attn_setup():
        import jax, jax.numpy as jnp
        import numpy as np
        N_HEADS = 16
        N_KV_HEADS = 4
        MAX_TIMESCALE = 10000.0

        def rms_norm(x):
            var = jnp.mean(jnp.square(x.astype(jnp.float32)), axis=-1, keepdims=True)
            return (x * jax.lax.rsqrt(var + 1e-06)).astype(x.dtype)

        def rotate_half(x):
            x1, x2 = jnp.split(x, 2, axis=-1)
            return jnp.concatenate([-x2, x1], axis=-1)

        def sine_table(features, length):
            fraction = jnp.arange(0, features, 2, dtype=jnp.float32) / features
            inv_freq = 1.0 / MAX_TIMESCALE ** fraction
            sinusoid = jnp.arange(length, dtype=jnp.float32)[:, None] * inv_freq[None, :]
            sinusoid = jnp.concatenate([sinusoid, sinusoid], axis=-1)
            return (jnp.sin(sinusoid), jnp.cos(sinusoid))
        key = jax.random.key(seed)
        ks = jax.random.split(key, 5)
        B, T, C = (2, 128, 256)
        N, K = (N_HEADS, N_KV_HEADS)
        H = C // N
        init_std = np.sqrt(2.0 / (5.0 * C))
        wang_std = 2.0 / 24 / np.sqrt(N * H)
        x = jax.random.normal(ks[0], (B, T, C), dtype=jnp.float32)
        q_kernel = jax.random.normal(ks[1], (C, N * H), dtype=jnp.float32) * init_std
        k_kernel = jax.random.normal(ks[2], (C, K * H), dtype=jnp.float32) * init_std
        v_kernel = jax.random.normal(ks[3], (C, K * H), dtype=jnp.float32) * init_std
        out_kernel = jax.random.normal(ks[4], (N * H, C), dtype=jnp.float32) * wang_std
        return {'x': x, 'q_kernel': q_kernel, 'k_kernel': k_kernel, 'v_kernel': v_kernel, 'out_kernel': out_kernel}
    _L0_attn_in = _L0_attn_setup()

    def _L0_ffn_setup():
        import jax, jax.numpy as jnp
        import numpy as np
        E, H, I = (8, 256, 512)
        TOP_K = 1
        B, S = (1, 256)
        key = jax.random.key(seed)
        ks = jax.random.split(key, 7)
        std = 0.02
        return {'hidden_states': jax.random.normal(ks[0], (B, S, H), dtype=jnp.float32), 'router_w': jax.random.normal(ks[1], (E, H), dtype=jnp.float32) * std, 'gate_up_proj': jax.random.normal(ks[2], (E, H, 2 * I), dtype=jnp.float32) * std, 'down_proj': jax.random.normal(ks[3], (E, I, H), dtype=jnp.float32) * std, 'shared_gate_w': jax.random.normal(ks[4], (H, I), dtype=jnp.float32) * std, 'shared_up_w': jax.random.normal(ks[5], (H, I), dtype=jnp.float32) * std, 'shared_down_w': jax.random.normal(ks[6], (I, H), dtype=jnp.float32) * std}
    _L0_ffn_in = _L0_ffn_setup()

    def _L1_attn_setup():
        import jax, jax.numpy as jnp
        import numpy as np
        HIDDEN = 256
        NUM_HEADS = 16
        HEAD_DIM = HIDDEN // NUM_HEADS
        key = jax.random.key(seed)
        ks = jax.random.split(key, 5)
        B, S, H = (2, 256, HIDDEN)
        qkv_bound = float(np.sqrt(6.0 / (H + 3 * H)))
        out_bound = float(np.sqrt(6.0 / (H + H)))
        return {'x': jax.random.normal(ks[0], (B, S, H), dtype=jnp.float32), 'W_qkv': jax.random.uniform(ks[1], (3 * H, H), minval=-qkv_bound, maxval=qkv_bound, dtype=jnp.float32), 'b_qkv': jnp.zeros((3 * H,), dtype=jnp.float32), 'W_out': jax.random.uniform(ks[2], (H, H), minval=-out_bound, maxval=out_bound, dtype=jnp.float32), 'b_out': jnp.zeros((H,), dtype=jnp.float32)}
    _L1_attn_in = _L1_attn_setup()

    def _L1_ffn_setup():
        import jax, jax.numpy as jnp
        import numpy as np
        BLOCK = 64

        def dequant4bit(q, scale):
            return (q.astype(jnp.float32) - 7.5) * jnp.repeat(scale, BLOCK, axis=1)
        key = jax.random.key(seed)
        ks = jax.random.split(key, 11)
        B, S, D, H, R = (4, 256, 256, 1024, 16)
        return {'x1': jax.random.normal(ks[0], (B, S, D), jnp.float32), 'w_up_q': jax.random.randint(ks[1], (H, D), 0, 16, dtype=jnp.int32), 'w_up_scale': jax.random.uniform(ks[2], (H, D // BLOCK), jnp.float32) * 0.02, 'b_up': jax.random.normal(ks[3], (H,), jnp.float32) * 0.01, 'w_up_lora_a': jax.random.normal(ks[4], (D, R), jnp.float32) * 0.02, 'w_up_lora_b': jax.random.normal(ks[5], (R, H), jnp.float32) * 0.02, 'w_down_q': jax.random.randint(ks[6], (D, H), 0, 16, dtype=jnp.int32), 'w_down_scale': jax.random.uniform(ks[7], (D, H // BLOCK), jnp.float32) * 0.02, 'b_down': jax.random.normal(ks[8], (D,), jnp.float32) * 0.01, 'w_down_lora_a': jax.random.normal(ks[9], (H, R), jnp.float32) * 0.02, 'w_down_lora_b': jax.random.normal(ks[10], (R, D), jnp.float32) * 0.02}
    _L1_ffn_in = _L1_ffn_setup()
    _d = {'L0_attn_x': _L0_attn_in['x'], 'L0_attn_q_kernel': _L0_attn_in['q_kernel'], 'L0_attn_k_kernel': _L0_attn_in['k_kernel'], 'L0_attn_v_kernel': _L0_attn_in['v_kernel'], 'L0_attn_out_kernel': _L0_attn_in['out_kernel'], 'L0_ffn_router_w': _L0_ffn_in['router_w'], 'L0_ffn_gate_up_proj': _L0_ffn_in['gate_up_proj'], 'L0_ffn_down_proj': _L0_ffn_in['down_proj'], 'L0_ffn_shared_gate_w': _L0_ffn_in['shared_gate_w'], 'L0_ffn_shared_up_w': _L0_ffn_in['shared_up_w'], 'L0_ffn_shared_down_w': _L0_ffn_in['shared_down_w'], 'L1_attn_W_qkv': _L1_attn_in['W_qkv'], 'L1_attn_b_qkv': _L1_attn_in['b_qkv'], 'L1_attn_W_out': _L1_attn_in['W_out'], 'L1_attn_b_out': _L1_attn_in['b_out'], 'L1_ffn_w_up_q': _L1_ffn_in['w_up_q'], 'L1_ffn_w_up_scale': _L1_ffn_in['w_up_scale'], 'L1_ffn_b_up': _L1_ffn_in['b_up'], 'L1_ffn_w_up_lora_a': _L1_ffn_in['w_up_lora_a'], 'L1_ffn_w_up_lora_b': _L1_ffn_in['w_up_lora_b'], 'L1_ffn_w_down_q': _L1_ffn_in['w_down_q'], 'L1_ffn_w_down_scale': _L1_ffn_in['w_down_scale'], 'L1_ffn_b_down': _L1_ffn_in['b_down'], 'L1_ffn_w_down_lora_a': _L1_ffn_in['w_down_lora_a'], 'L1_ffn_w_down_lora_b': _L1_ffn_in['w_down_lora_b']}
    _x0 = _d['L0_attn_x']
    _d['L0_attn_x'] = jax.random.normal(jax.random.fold_in(jax.random.key(seed), 1), (4, 512, 256), dtype=_x0.dtype)
    del _x0
    return _d

def reference(L0_attn_x, L0_attn_q_kernel, L0_attn_k_kernel, L0_attn_v_kernel, L0_attn_out_kernel, L0_ffn_router_w, L0_ffn_gate_up_proj, L0_ffn_down_proj, L0_ffn_shared_gate_w, L0_ffn_shared_up_w, L0_ffn_shared_down_w, L1_attn_W_qkv, L1_attn_b_qkv, L1_attn_W_out, L1_attn_b_out, L1_ffn_w_up_q, L1_ffn_w_up_scale, L1_ffn_b_up, L1_ffn_w_up_lora_a, L1_ffn_w_up_lora_b, L1_ffn_w_down_q, L1_ffn_w_down_scale, L1_ffn_b_down, L1_ffn_w_down_lora_a, L1_ffn_w_down_lora_b):

    def _L0_attn_ref(x, q_kernel, k_kernel, v_kernel, out_kernel):
        import jax, jax.numpy as jnp
        import numpy as np
        N_HEADS = 16
        N_KV_HEADS = 4
        MAX_TIMESCALE = 10000.0

        def rms_norm(x):
            var = jnp.mean(jnp.square(x.astype(jnp.float32)), axis=-1, keepdims=True)
            return (x * jax.lax.rsqrt(var + 1e-06)).astype(x.dtype)

        def rotate_half(x):
            x1, x2 = jnp.split(x, 2, axis=-1)
            return jnp.concatenate([-x2, x1], axis=-1)

        def sine_table(features, length):
            fraction = jnp.arange(0, features, 2, dtype=jnp.float32) / features
            inv_freq = 1.0 / MAX_TIMESCALE ** fraction
            sinusoid = jnp.arange(length, dtype=jnp.float32)[:, None] * inv_freq[None, :]
            sinusoid = jnp.concatenate([sinusoid, sinusoid], axis=-1)
            return (jnp.sin(sinusoid), jnp.cos(sinusoid))
        B, T, C = x.shape
        N, K = (N_HEADS, N_KV_HEADS)
        G = N // K
        H = C // N
        q = rms_norm(jnp.dot(x, q_kernel))
        k = rms_norm(jnp.dot(x, k_kernel))
        v = jnp.dot(x, v_kernel)
        q = q.reshape(B, T, K, G, H)
        k = k.reshape(B, T, K, H)
        v = v.reshape(B, T, K, H)
        sin, cos = sine_table(H, T)
        qcos = cos[None, :, None, None, :]
        qsin = sin[None, :, None, None, :]
        kcos = cos[None, :, None, :]
        ksin = sin[None, :, None, :]
        q = (q * qcos + rotate_half(q) * qsin).astype(x.dtype)
        k = (k * kcos + rotate_half(k) * ksin).astype(x.dtype)
        scale = jax.lax.rsqrt(jnp.array(H, dtype=jnp.float32)).astype(q.dtype)
        logits = jnp.einsum('btkgh,bskh->bkgts', q * scale, k)
        probs = jax.nn.softmax(logits.astype(jnp.float32), axis=-1).astype(logits.dtype)
        encoded = jnp.einsum('bkgts,bskh->btkgh', probs, v)
        encoded = encoded.reshape(B, T, N * H)
        return jnp.dot(encoded, out_kernel)

    def _L0_ffn_ref(hidden_states, router_w, gate_up_proj, down_proj, shared_gate_w, shared_up_w, shared_down_w):
        import jax, jax.numpy as jnp
        import numpy as np
        E, H, I = (8, 256, 512)
        TOP_K = 1
        B, S = (1, 256)
        orig_shape = hidden_states.shape
        x = hidden_states.reshape(-1, H)
        T = x.shape[0]
        logits = x @ router_w.T
        top_vals, top_idx = jax.lax.top_k(logits, TOP_K)
        scores = jnp.full_like(logits, -jnp.inf)
        scores = scores.at[jnp.arange(T)[:, None], top_idx].set(top_vals)
        scores = jax.nn.sigmoid(scores.astype(jnp.float32)).astype(logits.dtype)
        xr = x[None, :, :] * scores.T[:, :, None]
        gate_up = jnp.einsum('eth,ehf->etf', xr, gate_up_proj)
        gate, up = jnp.split(gate_up, 2, axis=-1)
        routed = jnp.einsum('etf,efh->eth', up * jax.nn.silu(gate), down_proj)
        routed_sum = routed.sum(axis=0)
        shared = jax.nn.silu(x @ shared_gate_w) * (x @ shared_up_w) @ shared_down_w
        return (shared + routed_sum).reshape(orig_shape)

    def _L1_attn_ref(x, W_qkv, b_qkv, W_out, b_out):
        import jax, jax.numpy as jnp
        import numpy as np
        HIDDEN = 256
        NUM_HEADS = 16
        HEAD_DIM = HIDDEN // NUM_HEADS
        B, S, H = x.shape
        qkv = x @ W_qkv.T + b_qkv
        q, k, v = jnp.split(qkv, 3, axis=-1)

        def to_heads(t):
            return t.reshape(B, S, NUM_HEADS, HEAD_DIM).transpose(0, 2, 1, 3)
        q, k, v = (to_heads(q), to_heads(k), to_heads(v))
        scale = HEAD_DIM ** (-0.5)
        scores = jnp.einsum('bnqd,bnkd->bnqk', q, k) * scale
        causal = jnp.triu(jnp.ones((S, S), dtype=bool), k=1)
        scores = jnp.where(causal, -jnp.inf, scores)
        attn = jax.nn.softmax(scores, axis=-1)
        out = jnp.einsum('bnqk,bnkd->bnqd', attn, v)
        out = out.transpose(0, 2, 1, 3).reshape(B, S, H)
        return out @ W_out.T + b_out

    def _L1_ffn_ref(x1, w_up_q, w_up_scale, b_up, w_up_lora_a, w_up_lora_b, w_down_q, w_down_scale, b_down, w_down_lora_a, w_down_lora_b):
        import jax, jax.numpy as jnp
        import numpy as np
        BLOCK = 64

        def dequant4bit(q, scale):
            return (q.astype(jnp.float32) - 7.5) * jnp.repeat(scale, BLOCK, axis=1)
        w_up = dequant4bit(w_up_q, w_up_scale).T
        y1 = x1 @ w_up + b_up + x1 @ w_up_lora_a @ w_up_lora_b
        x2 = jax.nn.relu(y1)
        w_down = dequant4bit(w_down_q, w_down_scale).T
        y2 = x2 @ w_down + b_down + x2 @ w_down_lora_a @ w_down_lora_b
        return y2
    x = L0_attn_x
    x = _layernorm(x + _L0_attn_ref(x, L0_attn_q_kernel, L0_attn_k_kernel, L0_attn_v_kernel, L0_attn_out_kernel), axis=-1)
    x = _layernorm(x + _L0_ffn_ref(x, L0_ffn_router_w, L0_ffn_gate_up_proj, L0_ffn_down_proj, L0_ffn_shared_gate_w, L0_ffn_shared_up_w, L0_ffn_shared_down_w), axis=-1)
    x = _layernorm(x + _L1_attn_ref(x, L1_attn_W_qkv, L1_attn_b_qkv, L1_attn_W_out, L1_attn_b_out), axis=-1)
    x = _layernorm(x + _L1_ffn_ref(x, L1_ffn_w_up_q, L1_ffn_w_up_scale, L1_ffn_b_up, L1_ffn_w_up_lora_a, L1_ffn_w_up_lora_b, L1_ffn_w_down_q, L1_ffn_w_down_scale, L1_ffn_b_down, L1_ffn_w_down_lora_a, L1_ffn_w_down_lora_b), axis=-1)
    return x

_drawn_inputs = setup_inputs


def setup_inputs(seed=0):
    import zlib

    import numpy as np

    out = dict(_drawn_inputs(seed))
    spreads = {'L1_attn_b_qkv': (0.0, 0.1), 'L1_attn_b_out': (0.0, 0.1)}
    factors = {'L0_attn_q_kernel': 8.0,
     'L0_attn_k_kernel': 8.0,
     'L0_attn_v_kernel': 8.0,
     'L0_attn_out_kernel': 8.0,
     'L0_ffn_router_w': 6.694,
     'L0_ffn_gate_up_proj': 6.237,
     'L0_ffn_down_proj': 6.223,
     'L1_ffn_b_up': 7.415,
     'L1_ffn_w_up_lora_a': 2.68,
     'L1_ffn_w_up_lora_b': 2.676,
     'L1_ffn_b_down': 8.0,
     'L1_ffn_w_down_lora_a': 2.767,
     'L1_ffn_w_down_lora_b': 2.77,
     'L0_ffn_shared_gate_w': 8.0,
     'L0_ffn_shared_up_w': 8.0,
     'L0_ffn_shared_down_w': 8.0}
    for name, (base, spread) in spreads.items():
        noise = np.random.default_rng([zlib.crc32(name.encode()), seed]).standard_normal(out[name].shape)
        drawn = base * np.exp(spread * noise) if base else spread * noise
        out[name] = jnp.asarray(drawn.astype(out[name].dtype))
    for name, factor in factors.items():
        out[name] = (out[name] * factor).astype(out[name].dtype)
    return out
```

```python
from contextlib import ExitStack

import numpy as np

import concourse.bass as bass
from concourse import mybir

F32 = mybir.dt.float32
BF16 = mybir.dt.bfloat16
I32 = mybir.dt.int32
U32 = mybir.dt.uint32
ALU = mybir.AluOpType
ACT = mybir.ActivationFunctionType
AX = mybir.AxisListType

P = 128
B = 4
S = 512
C = 256
NC_ = C // P
NT = S // P
TT = B * NT
NH = 16
HD = C // NH
KV0 = 4
QK0 = C + KV0 * HD
QKV0 = C + 2 * KV0 * HD
E = 8
FE = 512
NF = FE // P
MT = TT + E - 1
HID = 1024
NK = HID // P
RANK = 16
BLOCK = 64
HG = NH // 4
Q_PARTS = (0, 0, 0, 1, 1, 2)
K_PARTS = (0, 1, 2, 0, 1, 0)
STACK = 6 * HD
UNITS = 3
LN_EPS = 1e-5
RMS_EPS = 1e-6
NEG = -1e30

MAXES = [(qt, h, 4 // (qt + 1) if qt < 2 else 1) for qt in range(NT)
         for h in range(0, NH, 4 // (qt + 1) if qt < 2 else 1)]

A_START = """X0 X1 Q0 Q1 Q2 Q3 +X0 +X1 T0 T1 T2 V0 +Q0 +Q1 +Q2 +Q3"""
A_FIRST = """.rw0 | | | +T0 | | +T1 | | +T2 | | >X0 | >X1 | | | | | |"""
A_SECOND = """-F0 -F1 .V0 | -G0 -F2 -F3 +Q0 | -G1 -P0 | -P1 +Q1 | +Q2 | +Q3 | -N0 -N1 | -R0 -Sg0 | -Sg1 -Sg2 -Sg3 |
-Su0 | +T0 +T1 +T2 -Su1 | -Su2 | -Su3 | | -D0 | -D1 |"""
A_THIRD = """-F0 -F1 .V0 +X0 +X1 | -G0 -F2 -F3 +Q0 | -G1 -P0 | -P1 +Q1 | +Q2 | +Q3 | -N0 -N1 | | -Sg0 -Sg1 | -R0 -Sg2
-Sg3 | -Su0 | +T0 +T1 +T2 -Su1 | -Su2 | -Su3 | -D0 | -D1 |"""
A_LAST = """.V0 -F0 -F1 | -G0 -F2 -F3 | -G1 -P0 | | -P1 | | -N0 | -N1 -R0 -Sg0 | -Sg1 | -Sg2 | -Sg3 | -Su0 -Su1 |
-Su2 | -Su3 | -D0 | -D1 |"""
A_END = """-F0 -F1 -G0 -F2 -F3 -G1 -P0 -P1 -N0 -N1 -R0 RK0 -Sg0 -Sg1 -Sg2 -Sg3 -Su0 -Su1 -Su2 -Su3 -D0 -D1 ID0 Wq0
Wq1 Wq2 Wo0"""
C_START = """Wb0 Wat0 Wat1 Wat2 Wu0 Wul0 Wu1 Wul1 Wu2 Wul2 Wu3 Wul3 cL0 Wd0 Wd1 cX0 cL1 Wd2 Wd3 cX1 cQ0 cQ1 cK0 cQ2
cK1 cQ3 cK2 cV0 cK3 cV1 Wdl0 Wdl1 +cL0 Wdl2 +cX0 +cL1 Wdl3 +cX1 +cQ0 m m +cK0 m m +cQ1 m m m m +cK1 m m
+cQ2 m m m +cK2 m m +cQ3 m m m m +cK3 m m m m m m +cV0 m m m m m m m m m m m m m m m m m m m cM0 +cV1"""
C_FIRST = """| | +m +m | +m +m +m +m | +m +m | +m +m +m +m | +m +m +m | +m +m +m | +m +m +m +m | +m +m +m | +m +m +m |
+m +m +m | +m +m +m +m | +m +m +m +m +m +m +m +m +m | +cM0 >cL0 | >cL1 |"""
C_SECOND = """-cF0 -cF1 +cX0 | -cG0 -cF2 -cF3 +cX1 +cQ0 | -cG1 +cK0 -cP0 +cQ1 | -cP1 +cK1 +cQ2 | +cQ3 +cK2 =cO0 +cK3 |
+cV0 +cV1 =cO1 | -cN0 -cN1 -cH0 -cH1 >cL0 | -cH2 +m +m -cH3 >cL1 +m +m -cH4 +m +m | -cH5 +m +m -cH6 +m +m
+m -cH7 +m | +m +m +m | +m +m +m -cD0 +m +m +m | +m +m -cD1 +m +m +m | +m +m +m -cD2 +m +m +m | +m +m +m
+m +m +m +m +m +m +m +m +m | +cM0 -cD3 | |"""
C_THIRD = """-cF0 -cF1 +cX0 | -cG0 -cF2 -cF3 +cX1 +cQ0 | -cG1 +cK0 -cP0 +cQ1 | -cP1 +cK1 +cQ2 | +cQ3 +cK2 =cO0 +cK3 |
+cV0 +cV1 =cO1 | -cN0 -cN1 -cH0 -cH1 | -cH2 -cH3 +m +m +m +m -cH4 +m +m | -cH5 +m +m -cH6 +m +m | +m -cH7
+m +m +m +m | +m +m +m -cD0 +m +m +m | +m +m -cD1 +m +m +m | +m +m -cD2 +m +m +m | +m +m +m +m +m +m +m
+m +m +m +m +m +m | +cM0 -cD3 | |"""
C_LAST = """-cF0 -cF1 | -cG0 -cF2 | -cF3 -cG1 -cP0 | -cP1 =cO0 | =cO1 -cN0 -cN1 | -cH0 -cH1 | -cH2 | -cH3 | -cH4 |
-cH5 | | -cH6 | -cH7 | -cD0 | -cD1 -cO0 | -cD2 -cD3 |"""
C_END = """-cF0 -cF1 -cG0 -cF2 -cF3 -cG1 -cP0 -cP1 -cN0 -cI0 -cI1 -cI2 -cI3 -cI4 -cN1 -cI5 -cI6 -cI7 =cO1 -cI8 -cI9
-cI10 -cI11 -cD0 -cI12 -cI13 -cD1 -cI14 -cI15 -cO0 -cD2 -cD3 -cO1"""
DVE_ONLY = ("V", "cK", "cL", "cO")


def expand(names, b, m):
    steps = []
    for x in names.split():
        sign = x[0] if x[0] in "=-.+>" else ""
        to = b + {"=": -2, "-": -1, ".": 0, "+": 1, ">": 2}[sign] if sign else 0
        x = x[len(sign):]
        if x == "m":
            if to < B:
                steps.append(("max", to, m[0]))
            m[0] += 1
        elif 0 <= to < B:
            kind = x.rstrip("0123456789")
            steps.append((kind, to, int(x[len(kind):])))
    return steps


def attention_order(fills, name):
    steps = []
    last = B * NT * HG - 1
    for b, fill in enumerate(fills):
        m = [0]
        *fill, rest = fill.split("|")
        assert len(fill) == NT * HG and not rest.strip()
        for i, names in enumerate(fill):
            k = b * NT * HG + i
            if k == 0:
                steps.append((name + "S", b, i))
            if k < last:
                steps.append((name + "S", (k + 1) // (NT * HG), (k + 1) % (NT * HG)))
            steps += expand(names, b, m)
            steps.append((name + "P", b, i))
        assert m[0] in (0, len(MAXES)), m
    return steps


def a_order():
    return (expand(A_START, 0, [0]) + attention_order([A_FIRST, A_SECOND, A_THIRD, A_LAST], "att")
            + expand(A_END, B, [0]))


def c_order():
    return (expand(C_START, 0, [0]) + attention_order([C_FIRST, C_SECOND, C_THIRD, C_LAST], "catt")
            + expand(C_END, B, [0]))


def post_ln_layers(nc, ins, out):
    a_steps, c_steps = a_order(), c_order()
    shared = [s for s in a_steps + c_steps if "att" not in s[0] and s[0] not in DVE_ONLY]
    unit_no = {s: n for n, s in enumerate(shared)}

    with ExitStack() as ctx:
        words = (nc.sbuf_bytes_remaining() if callable(nc.sbuf_bytes_remaining) else nc.sbuf_bytes_remaining) // 32 * 8 - 8
        arena = ctx.enter_context(nc.sbuf_tensor("arena", [P, words], F32))
        ps = ctx.enter_context(nc.psum_tensor("ps", [P, 8, 512], F32))
        top = [0]

        def place(shape, dt=F32):
            n = int(np.prod(shape)) * (2 if dt == BF16 else 4)
            n = (n + 31) // 32 * 8
            at = top[0]
            top[0] += n
            assert top[0] <= words, (top[0] * 4, words * 4)
            ap = arena[:, at:at + n]
            if dt != F32:
                ap = ap.bitcast(dt)
            ap = ap[:, 0:int(np.prod(shape))]
            if len(shape) > 1:
                names = "abcd"[:len(shape)]
                ap = ap.rearrange(f"p ({' '.join(names)}) -> p {' '.join(names)}",
                                  **{x: s for x, s in zip(names[1:], shape[1:])})
            return ap

        ident = place([P])
        identb = place([P], BF16)
        upper = place([P])
        ones = place([P])
        negmask = place([P], BF16)
        cosb = place([NT, HD])
        sinb = place([NT, HD])
        iotae = place([E])
        iotaj = place([24])
        tok_id = place([TT])
        x_sb = place([TT, C])
        slot_i = place([TT], I32)
        gu_at = top[0]
        gu = place([E, NC_, 2 * FE])
        probs1 = gu[:, E - 1, :, :].rearrange("p c (a n) -> p (c a) n", a=2)
        dn_at = top[0]
        dn = place([E, NF, C])
        after_dn = top[0]
        top[0] = dn_at
        q_stack = place([2, NH, S], BF16)
        assert top[0] <= after_dn
        top[0] = after_dn
        zone = top[0]
        x_t = place([NC_, S])
        a_t = place([NC_, S])
        qkv = place([NT, QKV0])
        rot = place([NT, QK0])
        o_sb = place([HG, S])
        attn = place([2, C])
        zone_end = top[0]
        probs0 = place([4, S])
        xs = place([NT, C])
        w_qkv = place([NC_, QKV0])
        w_o = place([NC_, C])
        rw_t = place([NC_, E])
        s_gate = place([NC_, FE])
        s_up = place([NC_, FE])
        s_down = place([NF, C])
        k_stack = place([2, KV0, S], BF16)
        parts = place([2, 3, S], BF16)
        resid = place([S])
        v_aug = place([NT, KV0, 2 * HD])
        x1_t = place([NC_, S])
        h_t = place([NF, S])
        n_rw = place([C])
        ss = place([2, NT])
        logits = place([NT, E])
        top8 = place([NT, 8])
        idx8 = place([NT, 8], U32)
        idxf = place([NT, 1])
        score = place([NT])
        score_e = place([NT])
        id_row = place([P])
        small_at = top[0]
        rs = place([8])
        rs_a = place([8])
        rs_b = place([8])
        st = place([NT, 6])
        mv = place([NT, 2])
        rden = place([NH])
        onehot = place([TT, E])
        ids = place([MT], I32)
        end_a = top[0]
        top[0] = zone
        cnt_a = place([TT, E])
        cnt_b = place([TT, E])
        rank = place([TT, E])
        slotf = place([TT])
        nt_i = place([E], I32)
        ntf = place([E])
        end_x = place([E])
        end_y = place([E])
        base = place([E])
        cmp = place([24, E])
        ej = place([24])
        ej_i = place([24], I32)
        xg = place([2, C])
        xg_t = place([2, NC_, P])
        sg = place([2, FE])
        hh = place([2, FE])
        hh_t = place([2, NF, P])
        yg = place([2, C])
        assert top[0] <= zone_end, (top[0], zone_end)
        top[0] = zone_end
        w1_qkv = place([NC_, 3 * C])
        w1_o = place([NC_, C])
        w_up = place([NC_, HID])
        w_dn = place([NK, C])
        b_qk = place([4])
        b_up = place([NK])
        raw_at = top[0]
        n_qkv = place([6, C])
        n_o = place([2, C])
        n_up = place([NK, C])
        n_ups = place([NK, C // BLOCK])
        n_dn = place([2, HID])
        n_dns = place([2, HID // BLOCK])
        n_ua = place([2, RANK])
        n_ub = place([HID])
        n_da = place([NK, RANK])
        n_db = place([C])
        ua_t = place([C])
        da_t = place([HID])
        raw_end = top[0]
        assert top[0] <= small_at, (top[0], small_at)
        n_b = onehot.rearrange("p t e -> p (t e)")
        top[0] = gu_at
        cq_stack = place([2, NH, S], BF16)
        ck_stack = place([2, NH, S], BF16)
        assert top[0] <= dn_at
        top[0] = dn_at
        cv_aug = place([2, NT, NH, 2 * HD])
        hid_t = place([NK, S])
        assert top[0] <= after_dn
        top[0] = zone
        bv_b = place([C])
        bo_b = place([C])
        bd_b = place([C])
        yrow = place([NT, C])
        c_x_t = place([NC_, S])
        c_a_t = place([NC_, S])
        c_x3_t = place([NC_, S])
        y2 = place([NT, C])
        mneg = place([NT, NH])
        mparts = place([NT, 2, NH], BF16)
        m_t = place([S], BF16)
        cattn = place([2, C])
        cresid = place([S])
        assert top[0] <= zone_end, (top[0], zone_end)
        top[0] = raw_at
        cparts = place([2, 3, S], BF16)
        qf = [place([S])]
        cprobs = place([2, 4, S])
        co_sb = place([HG, S])
        assert top[0] <= raw_end
        top[0] = raw_end
        qf += [place([S])]
        assert top[0] <= small_at, (top[0], small_at)
        top[0] = end_a

        scr = nc.dram_tensor("parts_dram", [2 * B, 3, 2 * C, S], BF16).ap()
        xs_dram = nc.dram_tensor("xs_dram", [TT * P, C], F32).ap()
        id_dram = nc.dram_tensor("id_dram", [MT * P, 1], F32).ap()
        yg_dram = nc.dram_tensor("yg_dram", [MT * P, C], F32).ap()

        def sem(name):
            return ctx.enter_context(nc.semaphore(name))

        s_ident = sem("identity_loaded")
        s_const = sem("rope_tables_and_triangle_loaded")
        s_small = sem("small_operands_loaded")
        s_x = [sem(f"x_loaded{b}") for b in range(B)]
        s_w0 = sem("attn_weights_loaded")
        s_w1 = sem("shared_weights_loaded")
        s_gu = sem("gate_up_loaded")
        s_dn = sem("down_loaded")
        s_zero = sem("slots_zeroed")
        s_zrow = sem("zero_row_ready")
        s_xs = sem("xs_in_dram")
        s_idr = sem("ids_loaded")
        moe_in = sem("moe_scratch_free")
        s_ones = sem("ones_ready")
        unit_full = [sem(f"unit_full{i}") for i in range(UNITS)]
        unit_free = [sem(f"unit_free{i}") for i in range(UNITS)]
        rope_done = sem("rope_done")
        v_ready = sem("v_ready")
        part1 = sem("part1_ready")
        parts_ready = sem("parts_ready")
        s_scr = [sem(f"parts_in_dram{i}") for i in range(2)]
        s_stack = [sem(f"stacks_loaded{i}") for i in range(2)]
        s_full = [sem(f"scores_full{i}") for i in range(2)]
        exp_done = [sem(f"exp_done{i}") for i in range(2)]
        masked = sem("probs_masked")
        pv_done = sem("pv_done")
        o_evac = sem("o_evacuated")
        x1_ready = sem("x1_ready")
        silu_done = sem("silu_done")
        topped = sem("top_ready")
        exp_sc = sem("score_exp_ready")
        score_rdy = sem("score_ready")
        xs_ready = sem("xs_ready")
        xsum_ready = sem("x_plus_shared_ready")
        dve = sem("dve_chain")
        actc = sem("act_chain")
        poolc = sem("pool_chain")
        slots_ready = sem("slots_ready")
        experts_ready = sem("experts_ready")
        s_scat = sem("rows_scattered")
        xg_in = [sem(f"xg_loaded{i}") for i in range(2)]
        xgt_ps = sem("xg_transposed")
        xgt_sb = sem("xgT_ready")
        g_full = sem("gate_full")
        u_full = sem("up_full")
        sg_ready = sem("gate_silu_ready")
        h_done = sem("h_ready")
        ht_ps = sem("h_transposed")
        ht_sb = sem("hT_ready")
        y_full = sem("expert_out_full")
        y_sb = sem("expert_out_ready")
        y_st = [sem(f"expert_out_stored{i}") for i in range(2)]
        s_proj = sem("layer1_projections_loaded")
        s_nat = sem("layer1_raw_loaded")
        s_bias = sem("layer1_bias_loaded")
        deq = sem("dequantised")
        bqk_ready = sem("qk_bias_ready")
        gathered = sem("rows_gathered")
        x2_ready = sem("x2_ready")
        qf_ready = sem("qk_biased")
        cparts_ready = sem("cparts_ready")
        cs_scr = [sem(f"cparts_in_dram{i}") for i in range(2)]
        cs_stack = [sem(f"cstacks_loaded{i}") for i in range(2)]
        mx_full = [sem(f"max_scores_full{i}") for i in range(2)]
        mx_done = [sem(f"max_done{i}") for i in range(2)]
        m_parts = sem("max_parts_ready")
        s_m = sem("max_rows_loaded")
        kones = sem("k_ones_ready")
        x3_ready = sem("x3_ready")
        y_ready = sem("y_ready")
        s_out = sem("out_stored")

        def bank(step):
            return ps[:, 8 - UNITS + unit_no[step] % UNITS, :]

        def take(pe, step):
            u = unit_no[step]
            if u >= UNITS:
                pe.wait_ge(unit_free[u % UNITS], u // UNITS)
            return ps[:, 8 - UNITS + u % UNITS, :]

        def filled(eng, step):
            u = unit_no[step]
            eng.wait_ge(unit_full[u % UNITS], u // UNITS + 1)
            return ps[:, 8 - UNITS + u % UNITS, :]

        def consumed(eng, step):
            u = unit_no[step]
            eng.wait_ge(unit_free[u % UNITS], u // UNITS + 1)

        def full_of(step):
            return unit_full[unit_no[step] % UNITS]

        def free_of(step):
            return unit_free[unit_no[step] % UNITS]

        block = ctx.enter_context(nc.Block())
        head0, headc = NT * HG, NT * HG

        @block.sync
        def _(sp):
            x_rows = ins["x"].rearrange("b (t p) c -> b p t c", p=P)
            sp.dma_start(ident, ins["ident"]).then_inc(s_ident, 16)
            sp.dma_start(x_sb[:, 0:NT, :], x_rows[0]).then_inc(s_x[0], 16)
            sp.dma_start(w_qkv[:, :, 0:C], ins["q_kernel"].rearrange("(c p) n -> p c n", p=P)).then_inc(s_w0, 16)
            sp.dma_start(w_qkv[:, :, C:QK0], ins["k_kernel"].rearrange("(c p) n -> p c n", p=P)).then_inc(s_w0, 16)
            sp.dma_start(w_qkv[:, :, QK0:QKV0], ins["v_kernel"].rearrange("(c p) n -> p c n", p=P)).then_inc(s_w0, 16)
            for dst, name in ((cosb, "cos"), (sinb, "sin"), (upper, "upper")):
                sp.dma_start(dst, ins[name]).then_inc(s_const, 16)
            for dst, src in ((w_o, ins["out_kernel"].rearrange("(c p) n -> p c n", p=P)), (tok_id, ins["tok_id"]),
                             (n_rw[0:E], ins["router_w"]), (iotae, ins["iotae"]), (iotaj, ins["iotaj"])):
                sp.dma_start(dst, src).then_inc(s_small, 16)
            for b in range(1, B):
                sp.dma_start(x_sb[:, NT * b:NT * b + NT, :], x_rows[b]).then_inc(s_x[b], 16)
            sp.dma_start(s_gate, ins["shared_gate_w"].rearrange("(c p) n -> p c n", p=P)).then_inc(s_w1, 16)
            sp.dma_start(s_up, ins["shared_up_w"].rearrange("(c p) n -> p c n", p=P)).then_inc(s_w1, 16)
            sp.dma_start(s_down, ins["shared_down_w"].rearrange("(c p) n -> p c n", p=P)).then_inc(s_w1, 16)

            def stacks(step, qs, ks, nk, s_done):
                for j in range(6):
                    rows = slice(HD * j, HD * (j + 1))
                    sp.dma_start(qs[rows, :, :], scr[step, Q_PARTS[j], 0:C, :].rearrange("(h d) n -> d h n", d=HD))\
                      .then_inc(s_done, 16)
                    sp.dma_start(ks[rows, 0:nk, :],
                                 scr[step, K_PARTS[j], C:C + nk * HD, :].rearrange("(h d) n -> d h n", d=HD))\
                      .then_inc(s_done, 16)

            def layer0_stacks(b):
                for i in range(3):
                    w = P if i < 2 else KV0 * HD
                    sp.wait_ge(parts_ready, 3 * b + i + 1)
                    sp.dma_start(scr[b, :, P * i:P * i + w, :].rearrange("r p n -> p r n"), parts[0:w, i % 2, :, :])\
                      .then_inc(s_scr[i % 2], 16)
                sp.wait_ge(s_scr[0], 32 * (b + 1))
                sp.wait_ge(s_scr[1], 16 * (b + 1))
                if b >= 2:
                    sp.wait_ge(pv_done, head0 * (b - 1))
                stacks(b, q_stack[:, b % 2], k_stack[:, b % 2], KV0, s_stack[b % 2])

            def gate_up_load(experts):
                for e in experts:
                    sp.dma_start(gu[:, e, :, :], ins["gate_up_proj"][e].rearrange("(c p) n -> p c n", p=P))\
                      .then_inc(s_gu, 16)

            def xs_store(b):
                sp.wait_ge(xs_ready, b + 1)
                sp.dma_start(xs_dram[S * b:S * (b + 1), :].rearrange("(t p) c -> p t c", p=P), xs).then_inc(s_xs, 16)

            sp.wait_ge(s_zrow, 1)
            sp.dma_start(id_dram.rearrange("(j p) a -> j (p a)", p=P), id_row[0:MT, :]).then_inc(s_zero, 16)
            layer0_stacks(0)
            gate_up_load((0, 1, 2))
            layer0_stacks(1)
            gate_up_load((3, 4, 5))
            xs_store(0)
            layer0_stacks(2)
            gate_up_load((6,))
            xs_store(1)
            layer0_stacks(3)
            xs_store(2)
            sp.wait_ge(pv_done, head0 * B)
            gate_up_load((7,))
            for e in range(E):
                sp.dma_start(dn[:, e, :, :], ins["down_proj"][e].rearrange("(f p) n -> p f n", p=P)).then_inc(s_dn, 16)
            xs_store(3)
            sp.wait_ge(s_scat, 16 * TT)
            sp.dma_start(id_row[0:MT, :], id_dram.rearrange("(j p) a -> j (p a)", p=P)).then_inc(s_idr, 16)

            consumed(sp, ("D", B - 1, 0))
            consumed(sp, ("D", B - 1, 1))
            sp.dma_start(n_qkv, ins["W_qkv"].rearrange("(r p) n -> p r n", p=P)).then_inc(s_proj, 16)
            sp.dma_start(n_o, ins["W_out"].rearrange("(r p) n -> p r n", p=P)).then_inc(s_proj, 16)
            for dst, src in ((n_up.bitcast(I32), ins["w_up_q"].rearrange("(r p) n -> p r n", p=P)),
                             (n_ups, ins["w_up_scale"].rearrange("(r p) n -> p r n", p=P)),
                             (n_dn.bitcast(I32), ins["w_down_q"].rearrange("(r p) n -> p r n", p=P)),
                             (n_dns, ins["w_down_scale"].rearrange("(r p) n -> p r n", p=P)),
                             (n_ua, ins["w_up_lora_a"].rearrange("(r p) n -> p r n", p=P)),
                             (n_ub[0:RANK], ins["w_up_lora_b"]),
                             (n_da, ins["w_down_lora_a"].rearrange("(r p) n -> p r n", p=P)),
                             (n_db[0:RANK], ins["w_down_lora_b"]),
                             (n_b[0:4], ins["b_qkv"][0:2 * C].rearrange("(r p) -> r p", p=P)),
                             (n_b[4:4 + NK], ins["b_up"].rearrange("(r p) -> r p", p=P))):
                sp.dma_start(dst, src).then_inc(s_nat, 16)

            def y_store(j, half):
                sp.wait_ge(y_sb, j + 1)
                sp.dma_start(yg_dram[bass.ds(j * P, P), :], yg[:, half, :]).then_inc(y_st[half], 16)

            y_store(0, 0)
            with sp.Fori(0, 10) as i:
                for d in (1, 2):
                    y_store(2 * i + d, d % 2)
            y_store(21, 1)
            y_store(22, 0)

            sp.wait_ge(y_full, MT)
            for dst, src in ((bv_b, ins["b_qkv"][2 * C:3 * C]), (bo_b, ins["b_out"]), (bd_b, ins["b_down"])):
                sp.dma_start(dst, src.rearrange("(a n) -> a n", a=1).to_broadcast([P, C])).then_inc(s_bias, 16)

            for step in c_steps:
                n, b, i = step
                if n == "cK":
                    sp.wait_ge(cparts_ready, 4 * b + i + 1)
                    sp.dma_start(scr[B + b, :, P * i:P * (i + 1), :].rearrange("r p n -> p r n"), cparts[:, i % 2, :, :])\
                      .then_inc(cs_scr[i % 2], 16)
                    if i == 3:
                        sp.wait_ge(cs_scr[0], 32 * (b + 1))
                        sp.wait_ge(cs_scr[1], 32 * (b + 1))
                        if b >= 2:
                            sp.wait_ge(pv_done, head0 * B + headc * (b - 1))
                        stacks(B + b, cq_stack[:, b % 2], ck_stack[:, b % 2], NH, cs_stack[b % 2])
                elif n == "cM":
                    consumed(sp, step)
                    for j in range(2):
                        sp.dma_start(cq_stack[STACK + j:STACK + j + 1, b % 2, :, :], m_t[NH * j:NH * (j + 1), :])\
                          .then_inc(s_m, 16)
                elif n == "cO":
                    sp.wait_ge(y_ready, 2 * b + i + 1)
                    sp.dma_start(out.rearrange("b (t p) c -> b p t c", p=P)[b][:, 2 * i:2 * i + 2, :],
                                 y2[:, 2 * i:2 * i + 2, :]).then_inc(s_out, 16)
            sp.wait_ge(s_out, 32 * B)

        @block.tensor
        def _(pe):
            def wide(step, pieces, inputs):
                dst = take(pe, step)
                for col, src, idn, rows in pieces:
                    n = src.shape[0]
                    last = nc.tensor.transpose(dst[0:rows, col:col + n], src, idn)
                last.then_inc(full_of(step), 1)

            def products(step, groups):
                dst = take(pe, step)
                for (rows, lo, hi), pairs in groups:
                    for n, (a, w) in enumerate(pairs):
                        last = nc.tensor.matmul(dst[0:rows, lo:hi], a, w, start=(n == 0), stop=(n == len(pairs) - 1))
                last.then_inc(full_of(step), 1)

            def cols(t):
                return slice(P * t, P * (t + 1))

            pe.wait_ge(s_ident, 16)
            pe.wait_ge(s_const, 48)
            pe.wait_ge(s_ones, 2)
            for step in a_steps:
                n, b, i = step
                if n == "rw":
                    pe.wait_ge(s_small, 80)
                    wide(step, [(E * c, n_rw[0:E, cols(c)], ident[0:E, 0:E], P) for c in range(2)], None)
                elif n == "X":
                    pe.wait_ge(s_x[b], 16)
                    wide(step, [(P * (2 * t + c), x_sb[:, NT * b + 2 * i + t, cols(c)], ident, P)
                                for t in range(2) for c in range(2)], None)
                elif n == "Q":
                    consumed(pe, ("X", b, 0))
                    consumed(pe, ("X", b, 1))
                    pe.wait_ge(s_w0, 48)
                    products(step, [((P, 0, QKV0), [(x_t[:, c, cols(i)], w_qkv[:, c, :]) for c in range(2)])])
                elif n == "T":
                    pe.wait_ge(rope_done, b + 1)
                    w = P if i < 2 else KV0 * HD
                    wide(step, [(P * t, rot[:, t, P * i:P * i + w], ident, w) for t in range(NT)], None)
                elif n == "attS":
                    hg, kt = i // NT, i % NT
                    if i == 0:
                        pe.wait_ge(s_stack[b % 2], 192 * (b // 2 + 1))
                    for g in range(4):
                        if g % 2 == 0 and head0 * b + i:
                            pe.wait_ge(exp_done[g // 2], head0 * b + i)
                        last = nc.tensor.matmul(ps[:, g, :], k_stack[0:STACK, b % 2, hg, cols(kt)],
                                                q_stack[0:STACK, b % 2, 4 * hg + g, :], start=True, stop=True)
                        if g % 2:
                            last.then_inc(s_full[g // 2], 1)
                elif n == "attP":
                    k = head0 * b + i
                    hg, kt = i // NT, i % NT
                    if i == 0:
                        pe.wait_ge(v_ready, b + 1)
                    if kt == 0 and HG * b + hg >= 1:
                        pe.wait_ge(o_evac, HG * b + hg)
                    for g in range(4):
                        if g % 2 == 0:
                            pe.wait_ge(exp_done[g // 2], k + 1)
                        last = nc.tensor.matmul(ps[32 * g:32 * g + 32, 4, :], v_aug[:, kt, hg, :],
                                                (probs0, probs1)[i % 2][:, g, :], start=(kt == 0), stop=(kt == NT - 1))
                    last.then_inc(pv_done, 1)
                elif n == "F":
                    pe.wait_ge(o_evac, HG * (b + 1))
                    wide(step, [(P * hg, o_sb[:, hg, cols(i)], ident, P) for hg in range(HG)], None)
                elif n == "G":
                    consumed(pe, ("F", b, 2 * i))
                    consumed(pe, ("F", b, 2 * i + 1))
                    wide(step, [(P * (2 * t + c), attn[:, t, cols(c)], ident, P)
                                for t in range(2) for c in range(2)], None)
                elif n == "P":
                    consumed(pe, ("G", b, i))
                    products(step, [((P, C * t, C * (t + 1)),
                                     [(a_t[:, c, cols(2 * i + t)], w_o[:, c, :]) for c in range(2)]) for t in range(2)])
                elif n == "N":
                    pe.wait_ge(x1_ready, 2 * b + i + 1)
                    wide(step, [(P * (2 * t + c), x_sb[:, NT * b + 2 * i + t, cols(c)], ident, P)
                                for t in range(2) for c in range(2)], None)
                elif n == "R":
                    consumed(pe, ("N", b, 0))
                    consumed(pe, ("N", b, 1))
                    products(step, [((P, E * t, E * (t + 1)), [(x1_t[:, c, cols(t)], rw_t[:, c, :]) for c in range(2)])
                                    for t in range(NT)])
                elif n in ("Sg", "Su"):
                    pe.wait_ge(s_w1, 48)
                    w = s_gate if n == "Sg" else s_up
                    products(step, [((P, 0, S), [(w[:, c, cols(i)], x1_t[:, c, :]) for c in range(2)])])
                elif n == "D":
                    for f in range(NF):
                        consumed(pe, ("Su", b, f))
                    products(step, [((P, C * t, C * (t + 1)), [(h_t[:, f, cols(2 * i + t)], s_down[:, f, :])
                                                              for f in range(NF)]) for t in range(2)])
                elif n == "RK":
                    consumed(pe, ("R", B - 1, 0))
                    pe.wait_ge(topped, 2 * B)
                    flat = onehot.rearrange("p t e -> p (t e)")
                    products(step, [((P, 0, P), [(upper, flat)]), ((P, P, 2 * P), [(ones, flat)])])
                elif n == "ID":
                    pe.wait_ge(s_idr, 16)
                    wide(step, [(0, id_row[0:MT, :], ident[0:MT, 0:MT], P)], None)
                elif n == "Wq":
                    pe.wait_ge(s_proj, 32)
                    wide(step, [(P * (2 * r + c), n_qkv[:, 2 * i + r, cols(c)], ident, P)
                                for r in range(2) for c in range(2)], None)
                elif n == "Wo":
                    wide(step, [(P * (2 * r + c), n_o[:, r, cols(c)], ident, P)
                                for r in range(2) for c in range(2)], None)

            def xg_turn(j, half, n, i):
                pe.wait_ge(xg_in[half], 16 * (i + 1))
                if n:
                    pe.wait_ge(xgt_sb, j)
                for c in range(2):
                    last = nc.tensor.transpose(ps[:, 4, cols(c)], xg[:, half, cols(c)], ident)
                last.then_inc(xgt_ps, 1)

            def gate_or_up(j, half, n, up, e):
                if not up:
                    pe.wait_ge(xgt_sb, j + 1)
                    if n >= 2:
                        pe.wait_ge(h_done, j - 1)
                for c in range(2):
                    last = nc.tensor.matmul(ps[:, 2 * half + up, :], xg_t[:, half, c, :],
                                            gu[:, e, c, FE * up:FE * (up + 1)], start=(c == 0), stop=(c == 1))
                last.then_inc(u_full if up else g_full, 1)

            def h_turn(j, half, n):
                pe.wait_ge(h_done, j + 1)
                if n:
                    pe.wait_ge(ht_sb, j)
                for f in range(NF):
                    last = nc.tensor.transpose(ps[:, 5, cols(f)], hh[:, half, cols(f)], ident)
                last.then_inc(ht_ps, 1)

            def down(j, half, n, e):
                pe.wait_ge(ht_sb, j + 1)
                if n >= 2:
                    pe.wait_ge(y_sb, j - 1)
                for f in range(NF):
                    last = nc.tensor.matmul(ps[:, 6 + half, 0:C], hh_t[:, half, f, :], dn[:, e, f, :],
                                            start=(f == 0), stop=(f == NF - 1))
                last.then_inc(y_full, 1)

            def expert(j):
                return pe.value_load(ej_i[0:1, bass.ds(j, 1)], min_val=0, max_val=E - 1)

            pe.wait_ge(experts_ready, 1)
            pe.wait_ge(s_gu, 16 * E)
            pe.wait_ge(s_dn, 16 * E)
            for last in (("Wq", 0, 1), ("Wq", 0, 2), ("Wo", 0, 0)):
                consumed(pe, last)
            e0 = expert(0)
            xg_turn(0, 0, 0, 0)
            gate_or_up(0, 0, 0, 0, e0)
            gate_or_up(0, 0, 0, 1, e0)
            xg_turn(1, 1, 1, 0)

            def tile_body(j, half, n, i, last=0):
                if last < 2:
                    e1 = expert(j + 1)
                    gate_or_up(j + 1, 1 - half, n + 1, 0, e1)
                h_turn(j, half, n)
                if last < 1:
                    xg_turn(j + 2, half, n + 2, i)
                if last < 2:
                    gate_or_up(j + 1, 1 - half, n + 1, 1, e1)
                down(j, half, n, expert(j))

            tile_body(0, 0, 0, 1)
            with pe.Fori(0, 10) as i:
                tile_body(2 * i + 1, 1, 2, i + 1)
                tile_body(2 * i + 2, 0, 2, i + 2)
            tile_body(21, 1, 2, 11, last=1)
            tile_body(22, 0, 2, 12, last=2)

            pe.wait_ge(y_sb, MT)
            pe.wait_ge(s_nat, 16 * 10)
            for step in c_steps:
                n, b, i = step
                if n == "Wat":
                    pieces = ([(P * c, n_ua[:, c, :], ident, RANK) for c in range(2)] if i == 0 else
                              [(P * r, n_da[:, 4 * (i - 1) + r, :], ident, RANK) for r in range(4)])
                    wide(step, pieces, None)
                elif n == "Wb":
                    wide(step, [(0, n_b[0:4 + NK, :], ident[0:4 + NK, 0:4 + NK], P)], None)
                elif n == "Wu":
                    pe.wait_ge(deq, 1)
                    c, half = i // 2, i % 2
                    wide(step, [(P * r, n_up[:, 4 * half + r, cols(c)], ident, P) for r in range(4)], None)
                elif n == "Wul":
                    c, half = i // 2, i % 2
                    consumed(pe, ("Wat", 0, 0))
                    products(step, [((P, 0, 512), [(ua_t[0:RANK, cols(c)], n_ub[0:RANK, 512 * half:512 * half + 512])])])
                elif n == "Wd":
                    pe.wait_ge(deq, 2)
                    wide(step, [(P * (2 * r + c), n_dn[:, c, cols(2 * i + r)], ident, P)
                                for r in range(2) for c in range(2)], None)
                elif n == "Wdl":
                    consumed(pe, ("Wat", 0, 2))
                    products(step, [((P, C * r, C * (r + 1)), [(da_t[0:RANK, cols(2 * i + r)], n_db[0:RANK, :])])
                                    for r in range(2)])
                elif n in ("cX", "cN"):
                    pe.wait_ge(x2_ready if n == "cX" else x3_ready, 2 * b + i + 1)
                    wide(step, [(P * (2 * t + c), x_sb[:, NT * b + 2 * i + t, cols(c)], ident, P)
                                for t in range(2) for c in range(2)], None)
                elif n == "cQ":
                    consumed(pe, ("cX", b, 0))
                    consumed(pe, ("cX", b, 1))
                    products(step, [((P, 0, S), [(w1_qkv[:, c, cols(i)], c_x_t[:, c, :]) for c in range(2)])])
                elif n == "cV":
                    products(step, [((P, C * t, C * (t + 1)),
                                     [(c_x_t[:, c, cols(2 * i + t)], w1_qkv[:, c, 2 * C:3 * C]) for c in range(2)])
                                    for t in range(2)])
                elif n == "max":
                    qt, h0, nh = MAXES[i]
                    if i == 0:
                        pe.wait_ge(cs_stack[b % 2], 192 * (b // 2 + 1))
                    dst = take(pe, step)
                    w = P * (qt + 1)
                    for g in range(nh):
                        nc.tensor.matmul(dst[:, w * g:w * (g + 1)], cq_stack[0:STACK, b % 2, h0 + g, cols(qt)],
                                         ck_stack[0:STACK, b % 2, h0 + g, 0:w], start=True, stop=True)
                        last = nc.tensor.matmul(dst[:, w * g + P * qt:w * (g + 1)], identb, negmask,
                                                start=False, stop=True, skip_group_check=True)
                    last.then_inc(full_of(step), 1)
                elif n == "cM":
                    pe.wait_ge(m_parts, b + 1)
                    dst = take(pe, step).bitcast(BF16)
                    for t in range(NT):
                        last = nc.tensor.transpose(dst[0:2 * NH, cols(t)], mparts[:, t, :, :].rearrange("p a h -> p (a h)"),
                                                   identb)
                    last.then_inc(full_of(step), 1)
                elif n == "cattS":
                    hg, kt = i // NT, i % NT
                    k = head0 * B + headc * b + i
                    if i == 0:
                        pe.wait_ge(s_m, 32 * (b + 1))
                        pe.wait_ge(kones, 1)
                    for g in range(4):
                        h = 4 * hg + g
                        if g % 2 == 0:
                            pe.wait_ge(exp_done[g // 2], k)
                        last = nc.tensor.matmul(ps[:, g, P * kt:S], ck_stack[0:STACK + 2, b % 2, h, cols(kt)],
                                                cq_stack[0:STACK + 2, b % 2, h, P * kt:S], start=True, stop=True)
                        if g % 2:
                            last.then_inc(s_full[g // 2], 1)
                elif n == "cattP":
                    hg, kt = i // NT, i % NT
                    if i == 0:
                        consumed(pe, ("cV", b, 0))
                        consumed(pe, ("cV", b, 1))
                    if kt == 0:
                        pe.wait_ge(o_evac, HG * (B + b) + hg)
                    pe.wait_ge(masked, headc * b + i + 1)
                    for g in range(4):
                        last = nc.tensor.matmul(ps[32 * g:32 * g + 32, 4, P * kt:S],
                                                cv_aug[:, b % 2, kt, 4 * hg + g, :],
                                                cprobs[:, i % 2, g, P * kt:S], start=(kt == 0), stop=(kt == NT - 1))
                    last.then_inc(pv_done, 1)
                elif n == "cF":
                    pe.wait_ge(o_evac, HG * (B + b + 1))
                    wide(step, [(P * hg, co_sb[:, hg, cols(i)], ident, P) for hg in range(HG)], None)
                elif n == "cG":
                    consumed(pe, ("cF", b, 2 * i))
                    consumed(pe, ("cF", b, 2 * i + 1))
                    wide(step, [(P * (2 * t + c), cattn[:, t, cols(c)], ident, P)
                                for t in range(2) for c in range(2)], None)
                elif n == "cP":
                    consumed(pe, ("cG", b, i))
                    products(step, [((P, C * t, C * (t + 1)),
                                     [(c_a_t[:, c, cols(2 * i + t)], w1_o[:, c, :]) for c in range(2)])
                                    for t in range(2)])
                elif n == "cH":
                    consumed(pe, ("cN", b, 0))
                    consumed(pe, ("cN", b, 1))
                    products(step, [((P, 0, S), [(w_up[:, c, cols(i)], c_x3_t[:, c, :]) for c in range(2)])])
                elif n == "cI":
                    half, k = i // NK, i % NK
                    consumed(pe, ("cN", b, half))
                    tok = slice(C * half, C * half + C)
                    products(step, [((P, 0, C), [(w_up[:, c, cols(k)], c_x3_t[:, c, tok]) for c in range(2)])])
                elif n == "cD":
                    for k in range(NK):
                        consumed(pe, ("cI", b, NK * (i // 2) + k) if ("cI", b, 0) in unit_no else ("cH", b, k))
                    products(step, [((P, 0, C), [(hid_t[:, k, cols(i)], w_dn[:, k, :]) for k in range(NK)])])

        @block.scalar
        def _(act):
            copy = ACT.Copy
            for step in a_steps:
                n, b, i = step
                if n == "Q":
                    if i == 0 and b:
                        act.wait_ge(parts_ready, 3 * b)
                        act.wait_ge(v_ready, b)
                    src = filled(act, step)
                    nc.scalar.activation(rot[:, i, 0:C], src[:, 0:C], ACT.Square, accum_out=ss[:, 0, i:i + 1])
                    nc.scalar.activation(rot[:, i, C:QK0], src[:, C:QK0], ACT.Square, accum_out=ss[:, 1, i:i + 1])
                    nc.scalar.activation(qkv[:, i, :], src[:, 0:QKV0], copy).then_inc(free_of(step), 1)
                elif n == "T":
                    if 3 * b + i >= 2:
                        act.wait_ge(s_scr[i % 2], 32 * b if i == 0 else 16 * b if i == 1 else 32 * b + 16)
                    src = filled(act, step)
                    w = P if i < 2 else KV0 * HD
                    nc.scalar.activation(parts[0:w, i % 2, 0, :], src[0:w, :], copy).then_inc(part1, 1)
                elif n == "attS":
                    if head0 * b + i >= 2:
                        act.wait_ge(pv_done, head0 * b + i - 1)
                    probs = (probs0, probs1)[i % 2]
                    for p in range(2):
                        act.wait_ge(s_full[p], head0 * b + i + 1)
                        nc.scalar.activation(probs[:, 2 * p:2 * p + 2, :], ps[:, 2 * p:2 * p + 2, :], ACT.Exp)\
                          .then_inc(exp_done[p], 1)
                elif n == "attP" and i % NT == NT - 1:
                    act.wait_ge(pv_done, head0 * b + i + 1)
                    nc.scalar.activation(o_sb[:, i // NT, :], ps[:, 4, :], copy).then_inc(o_evac, 1)
                elif n in ("X", "G", "N"):
                    dst = {"X": x_t, "G": a_t, "N": x1_t}[n]
                    src = filled(act, step).rearrange("p (t c n) -> p t c n", t=2, c=2)
                    nc.scalar.activation(dst[:, :, 2 * P * i:2 * P * (i + 1)].rearrange("p c (t n) -> p t c n", t=2),
                                         src, copy).then_inc(free_of(step), 1)
                elif n == "R":
                    act.wait_ge(topped, 2 * b + 1)
                    nc.scalar.activation(score_e, top8[:, :, 0], ACT.Exp, scale=-1.0).then_inc(exp_sc, 1)
                elif n == "Sg":
                    src = filled(act, step)
                    if b and i == 0:
                        filled(act, ("D", b - 1, 0))
                        filled(act, ("D", b - 1, 1))
                    nc.scalar.activation(h_t[:, i, :], src, ACT.Silu).then_inc(free_of(step), 1)

            def silu_tile(j, half, n):
                act.wait_ge(g_full, j + 1)
                if n >= 2:
                    act.wait_ge(h_done, j - 1)
                nc.scalar.activation(sg[:, half, :], ps[:, 2 * half, :], ACT.Silu).then_inc(sg_ready, 1)

            def ht_tile(j, half, n):
                act.wait_ge(ht_ps, j + 1)
                if n >= 2:
                    act.wait_ge(y_full, j - 1)
                nc.scalar.activation(hh_t[:, half, :, :].rearrange("p f n -> p (f n)"), ps[:, 5, :], copy)\
                  .then_inc(ht_sb, 1)

            act.wait_ge(slots_ready, 1)
            silu_tile(0, 0, 0)
            silu_tile(1, 1, 1)
            ht_tile(0, 0, 0)
            with act.Fori(0, 10) as i:
                for d in (1, 2):
                    silu_tile(2 * i + (d + 1), 1 - d % 2, 2)
                    ht_tile(2 * i + d, d % 2, 2)
            silu_tile(22, 0, 2)
            ht_tile(21, 1, 2)
            ht_tile(22, 0, 2)

            for step in c_steps:
                n, b, i = step
                if n == "Wu":
                    c, half = i // 2, i % 2
                    nc.scalar.activation(w_up[:, c, 512 * half:512 * half + 512], filled(act, step), copy)\
                      .then_inc(free_of(step), 1)
                elif n == "Wd":
                    nc.scalar.activation(w_dn[:, 2 * i:2 * i + 2, :].rearrange("p r n -> p (r n)"), filled(act, step), copy)\
                      .then_inc(free_of(step), 1)
                elif n in ("cX", "cG", "cN"):
                    dst = {"cX": c_x_t, "cG": c_a_t, "cN": c_x3_t}[n]
                    src = filled(act, step).rearrange("p (t c n) -> p t c n", t=2, c=2)
                    nc.scalar.activation(dst[:, :, 2 * P * i:2 * P * (i + 1)].rearrange("p c (t n) -> p t c n", t=2),
                                         src, copy).then_inc(free_of(step), 1)
                elif n == "cQ":
                    src = filled(act, step)
                    if 4 * b + i >= 2:
                        act.wait_ge(cparts_ready, 4 * b + i - 1)
                    consumed(act, ("Wb", 0, 0))
                    act.wait_ge(bqk_ready, 1)
                    if 4 * b + i >= 2:
                        act.wait_ge(cs_scr[i % 2], 16 * ((4 * b + i) // 2))
                    for dst in (qf[i % 2], cparts[:, i % 2, 0, :]):
                        last = nc.scalar.activation(dst, src, ACT.Identity, bias=b_qk[:, i:i + 1],
                                                    scale=0.25 if i < 2 else 1.0)
                    last.then_inc(free_of(step), 1)
                elif n == "cattS":
                    kt = i % NT
                    if headc * b + i >= 2:
                        act.wait_ge(pv_done, head0 * B + headc * b + i - 1)
                    for p in range(2):
                        act.wait_ge(s_full[p], head0 * B + headc * b + i + 1)
                        nc.scalar.activation(cprobs[:, i % 2, 2 * p:2 * p + 2, P * kt:S], ps[:, 2 * p:2 * p + 2, P * kt:S],
                                             ACT.Exp).then_inc(exp_done[p], 1)
                elif n == "cattP" and i % NT == NT - 1:
                    act.wait_ge(pv_done, head0 * B + headc * b + i + 1)
                    nc.scalar.activation(co_sb[:, i // NT, :], ps[:, 4, :], copy).then_inc(o_evac, 1)
                elif n == "cM":
                    src = filled(act, step).bitcast(BF16)
                    if b:
                        act.wait_ge(s_m, 32 * b)
                    nc.scalar.activation(m_t[0:2 * NH, :], src[0:2 * NH, 0:S], copy).then_inc(free_of(step), 1)
                elif n == "cI":
                    half, k = i // NK, i % NK
                    nc.scalar.activation(hid_t[:, k, C * half:C * half + C], filled(act, step)[:, 0:C], ACT.Relu,
                                         bias=b_up[:, k:k + 1]).then_inc(free_of(step), 1)
                elif n == "cH":
                    nc.scalar.activation(hid_t[:, i, :], filled(act, step), ACT.Relu, bias=b_up[:, i:i + 1])\
                      .then_inc(free_of(step), 1)

        @block.vector
        def _(v):
            done = [0]

            def link(ins_):
                done[0] += 1
                ins_.then_inc(dve, 1)
                v.wait_ge(dve, done[0])

            def tick(ins_):
                done[0] += 1
                ins_.then_inc(dve, 1)

            def settle():
                v.wait_ge(dve, done[0])

            def rsqrt(x, y, t):
                link(nc.vector.tensor_scalar(y.bitcast(I32), x.bitcast(I32), -0.5, float(0x5F3759DF), ALU.mult, ALU.add))
                for _ in range(3):
                    link(nc.vector.tensor_tensor(t, y, y, ALU.mult))
                    link(nc.vector.scalar_tensor_tensor(out=t, in0=t, scalar=-0.5, in1=x, op0=ALU.mult, op1=ALU.mult))
                    link(nc.vector.scalar_tensor_tensor(out=y, in0=t, scalar=1.5, in1=y, op0=ALU.add, op1=ALU.mult))

            def stats(b, i, rows):
                for t in range(2):
                    tick(nc.vector.bn_stats(st[:, 2 * i + t, :], rows[:, t, :]))
                settle()
                for t in range(2):
                    tick(nc.vector.bn_aggr(mv[:, 2 * i + t, :], st[:, 2 * i + t, :]))
                settle()

            def normalise(dst, src, i, done_sem, n):
                half = mv[:, 2 * i:2 * i + 2, :]
                x, xh, y, t = rs_a[:, 0:2], rs_a[:, 2:4], rs[:, 0:2], rs_b[:, 0:2]
                tick(nc.vector.tensor_scalar(xh, half[:, :, 1], LN_EPS, -0.5, ALU.add, ALU.mult))
                link(nc.vector.tensor_scalar(x, half[:, :, 1], LN_EPS, None, ALU.add))
                link(nc.vector.tensor_scalar(y.bitcast(I32), x.bitcast(I32), -0.5, float(0x5F3759DF), ALU.mult, ALU.add))
                for _ in range(3):
                    for k in range(2):
                        tick(nc.vector.scalar_tensor_tensor(out=t[:, k:k + 1], in0=y[:, k:k + 1], scalar=xh[:, k:k + 1],
                                                            in1=y[:, k:k + 1], op0=ALU.mult, op1=ALU.mult))
                    settle()
                    link(nc.vector.scalar_tensor_tensor(out=y, in0=t, scalar=1.5, in1=y, op0=ALU.add, op1=ALU.mult))
                tick(nc.vector.tensor_scalar(dst[:, 0, :], src[:, 0, :], half[:, 0, 0:1], rs[:, 0:1], ALU.subtract, ALU.mult))
                nc.vector.tensor_scalar(dst[:, 1, :], src[:, 1, :], half[:, 1, 0:1], rs[:, 1:2], ALU.subtract, ALU.mult)\
                  .then_inc(done_sem, 1)
                settle()
                v.wait_ge(done_sem, n)

            def heads(src, dst, r, step):
                wide = src.rearrange("p (h r) -> p h r", r=2 * HD)
                link(nc.vector.reciprocal(r, wide[:, :, HD]))
                nc.vector.tensor_tensor(dst.rearrange("p (h d) -> p h d", d=HD), wide[:, :, 0:HD],
                                        r.unsqueeze(2).to_broadcast([P, NH, HD]), ALU.mult).then_inc(free_of(step), 1)

            nc.vector.memset(ones, 1.0).then_inc(s_ones, 1)
            nc.vector.memset(v_aug, 1.0).then_inc(s_ones, 1)
            nc.vector.memset(id_row[0:MT, :], 0.0).then_inc(s_zrow, 1)
            v.wait_ge(s_ones, 2)
            v.wait_ge(s_ident, 16)
            v.wait_ge(s_const, 48)
            tick(nc.vector.tensor_copy(identb, ident))
            link(nc.vector.tensor_scalar(negmask, upper, NEG, None, ALU.mult))
            for step in a_steps:
                n, b, i = step
                if n == "rw":
                    nc.vector.tensor_copy(rw_t, filled(v, step)[:, 0:2 * E].rearrange("p (c e) -> p c e", c=2))\
                      .then_inc(free_of(step), 1)
                elif n == "Q" and i == NT - 1:
                    for t in range(NT):
                        consumed(v, ("Q", b, t))
                    tick(nc.vector.tensor_scalar(rs_a[:, 0:NT], ss[:, 0, :], 1.0 / C, RMS_EPS, ALU.mult, ALU.add))
                    tick(nc.vector.tensor_scalar(rs_a[:, NT:2 * NT], ss[:, 1, :], 1.0 / (KV0 * HD), RMS_EPS, ALU.mult, ALU.add))
                    settle()
                    rsqrt(rs_a, rs, rs_b)
                    link(nc.vector.tensor_scalar(rs[:, 0:NT], rs[:, 0:NT], 0.25, None, ALU.mult))
                    qk = qkv[:, :, 0:QK0].rearrange("p t (h d) -> p t h d", d=HD)
                    rt = rot.rearrange("p t (h d) -> p t h d", d=HD)
                    hh2 = HD // 2
                    nhk = QK0 // HD
                    tick(nc.vector.tensor_tensor(rt[:, :, :, 0:hh2], qk[:, :, :, hh2:HD],
                                                 sinb[:, :, 0:hh2].unsqueeze(2).to_broadcast([P, NT, nhk, hh2]), ALU.mult))
                    link(nc.vector.tensor_tensor(rt[:, :, :, hh2:HD], qk[:, :, :, 0:hh2],
                                                 sinb[:, :, hh2:HD].unsqueeze(2).to_broadcast([P, NT, nhk, hh2]), ALU.mult))
                    link(nc.vector.tensor_tensor(qk, qk, cosb.unsqueeze(2).to_broadcast([P, NT, nhk, HD]), ALU.mult))
                    link(nc.vector.tensor_tensor(rot, rot, qkv[:, :, 0:QK0], ALU.add))
                    tick(nc.vector.tensor_tensor(rot[:, :, 0:C], rot[:, :, 0:C],
                                                 rs[:, 0:NT].unsqueeze(2).to_broadcast([P, NT, C]), ALU.mult))
                    nc.vector.tensor_tensor(rot[:, :, C:QK0], rot[:, :, C:QK0],
                                            rs[:, NT:2 * NT].unsqueeze(2).to_broadcast([P, NT, KV0 * HD]),
                                            ALU.mult).then_inc(rope_done, 1)
                    v.wait_ge(rope_done, b + 1)
                elif n == "V":
                    if b:
                        v.wait_ge(pv_done, head0 * b)
                    nc.vector.tensor_copy(v_aug[:, :, :, 0:HD], qkv[:, :, QK0:QKV0].rearrange("p t (h d) -> p t h d", d=HD))\
                      .then_inc(v_ready, 1)
                elif n == "T":
                    w = P if i < 2 else KV0 * HD
                    src = bank(step)
                    v.wait_ge(part1, 3 * b + i + 1)
                    settle()
                    v.wait_ge(parts_ready, 3 * b + i)
                    pt = parts[0:w, i % 2]
                    nc.vector.tensor_tensor(resid[0:w], src[0:w, :], pt[:, 0, :], ALU.subtract)\
                      .then_inc(free_of(step), 1)
                    consumed(v, step)
                    link(nc.vector.tensor_copy(pt[:, 1, :], resid[0:w]))
                    nc.vector.tensor_tensor(pt[:, 2, :], resid[0:w], pt[:, 1, :], ALU.subtract)\
                      .then_inc(parts_ready, 1)
                elif n == "F":
                    src = filled(v, step)
                    if i:
                        consumed(v, ("F", b, i - 1))
                    heads(src, attn[:, i % 2, :], rden, step)
                elif n == "P":
                    rows = x_sb[:, NT * b + 2 * i:NT * b + 2 * i + 2, :]
                    src = filled(v, step).rearrange("p (t n) -> p t n", t=2)
                    nc.vector.tensor_tensor(rows, src, rows, ALU.add).then_inc(free_of(step), 1)
                    consumed(v, step)
                    stats(b, i, rows)
                    normalise(rows, rows, i, x1_ready, 2 * b + i + 1)
                elif n == "R":
                    src = filled(v, step)[:, 0:NT * E].rearrange("p (t e) -> p t e", e=E)
                    nc.vector.tensor_copy(logits, src).then_inc(free_of(step), 1)
                    consumed(v, step)
                    for t in range(NT):
                        last = nc.vector.max(top8[:, t, :], logits[:, t, :])
                        if t < NT - 1:
                            tick(last)
                    last.then_inc(topped, 1)
                    v.wait_ge(topped, 2 * b + 1)
                    settle()
                    for t in range(NT):
                        tick(nc.vector.max_index(idx8[:, t, :], top8[:, t, :], logits[:, t, :]))
                    settle()
                    link(nc.vector.tensor_copy(idxf, idx8[:, :, 0:1]))
                    nc.vector.tensor_tensor(onehot[:, NT * b:NT * b + NT, :], iotae.unsqueeze(1).to_broadcast([P, NT, E]),
                                            idxf.to_broadcast([P, NT, E]), ALU.is_equal).then_inc(topped, 1)
                    v.wait_ge(exp_sc, b + 1)
                    link(nc.vector.tensor_scalar(score, score_e, 1.0, None, ALU.add))
                    link(nc.vector.reciprocal(score, score))
                    rows = slice(NT * b, NT * b + NT)
                    if b:
                        v.wait_ge(s_xs, 16 * b)
                    nc.vector.tensor_tensor(xs, x_sb[:, rows, :], score.unsqueeze(2).to_broadcast([P, NT, C]),
                                            ALU.mult).then_inc(xs_ready, 1)
                elif n == "Su":
                    src = filled(v, step)
                    consumed(v, ("Sg", b, i))
                    nc.vector.tensor_tensor(h_t[:, i, :], src, h_t[:, i, :], ALU.mult).then_inc(free_of(step), 1)
                elif n == "D":
                    rows = x_sb[:, NT * b + 2 * i:NT * b + 2 * i + 2, :]
                    src = filled(v, step).rearrange("p (t n) -> p t n", t=2)
                    v.wait_ge(xs_ready, b + 1)
                    nc.vector.tensor_tensor(rows, src, rows, ALU.add).then_inc(free_of(step), 1)
                elif n == "RK":
                    src = filled(v, step)
                    flat = "p t e -> p (t e)"
                    tick(nc.vector.tensor_copy(rank.rearrange(flat), src[:, 0:P]))
                    nc.vector.tensor_copy(cnt_a.rearrange(flat), src[:, P:2 * P]).then_inc(free_of(step), 1)
                    consumed(v, step)
                    settle()
                    a, z = cnt_a, cnt_b
                    for d in (1, 2, 4, 8):
                        tick(nc.vector.tensor_copy(z[:, 0:d, :], a[:, 0:d, :]))
                        link(nc.vector.tensor_tensor(z[:, d:TT, :], a[:, d:TT, :], a[:, 0:TT - d, :], ALU.add))
                        a, z = z, a
                    total = a[:, TT - 1, :]
                    link(nc.vector.tensor_scalar(nt_i, total, float(P - 1), None, ALU.add))
                    link(nc.vector.tensor_scalar(nt_i, nt_i, 7, None, ALU.arith_shift_right))
                    link(nc.vector.tensor_copy(ntf, nt_i))
                    link(nc.vector.tensor_copy(end_x, ntf))
                    p_, q_ = end_x, end_y
                    for d in (1, 2, 4):
                        tick(nc.vector.tensor_copy(q_[:, 0:d], p_[:, 0:d]))
                        link(nc.vector.tensor_tensor(q_[:, d:E], p_[:, d:E], p_[:, 0:E - d], ALU.add))
                        p_, q_ = q_, p_
                    link(nc.vector.tensor_tensor(base, p_, ntf, ALU.subtract))
                    link(nc.vector.tensor_scalar(base, base, float(P), None, ALU.mult))
                    link(nc.vector.tensor_tensor(rank[:, 1:TT, :], rank[:, 1:TT, :], a[:, 0:TT - 1, :], ALU.add))
                    link(nc.vector.tensor_tensor(rank, rank, base.unsqueeze(1).to_broadcast([P, TT, E]), ALU.add))
                    link(nc.vector.tensor_tensor(rank, rank, onehot, ALU.mult))
                    link(nc.vector.tensor_reduce(slotf, rank, AX.X, ALU.add))
                    nc.vector.tensor_copy(slot_i, slotf).then_inc(slots_ready, 1)
                    link(nc.vector.tensor_tensor(cmp, iotaj.unsqueeze(2).to_broadcast([P, 24, E]),
                                                 p_.unsqueeze(1).to_broadcast([P, 24, E]), ALU.is_ge))
                    link(nc.vector.tensor_reduce(ej, cmp, AX.X, ALU.add))
                    link(nc.vector.tensor_scalar(ej, ej, float(E - 1), None, ALU.min))
                    nc.vector.tensor_copy(ej_i, ej).then_inc(experts_ready, 1)
                elif n == "ID":
                    nc.vector.tensor_copy(ids, filled(v, step)[:, 0:MT]).then_inc(free_of(step), 1)
                elif n in ("Wq", "Wo"):
                    dst = w1_qkv[:, :, 2 * P * i:2 * P * (i + 1)] if n == "Wq" else w1_o
                    src = filled(v, step).rearrange("p (r c n) -> p r c n", r=2, c=2)
                    nc.vector.tensor_copy(dst.rearrange("p c (r n) -> p r c n", r=2), src).then_inc(free_of(step), 1)

            def xgt_tile(j, half, n):
                v.wait_ge(xgt_ps, j + 1)
                if n >= 2:
                    v.wait_ge(u_full, j - 1)
                nc.vector.tensor_copy(xg_t[:, half, :, :].rearrange("p c n -> p (c n)"), ps[:, 4, 0:C]).then_inc(xgt_sb, 1)

            def h_tile(j, half, n):
                v.wait_ge(sg_ready, j + 1)
                v.wait_ge(u_full, j + 1)
                if n >= 2:
                    v.wait_ge(ht_ps, j - 1)
                nc.vector.tensor_tensor(hh[:, half, :], ps[:, 2 * half + 1, :], sg[:, half, :], ALU.mult).then_inc(h_done, 1)

            def y_tile(j, half, n, i):
                v.wait_ge(y_full, j + 1)
                if n >= 2:
                    v.wait_ge(y_st[half], 16 * i)
                nc.vector.tensor_copy(yg[:, half, :], ps[:, 6 + half, 0:C]).then_inc(y_sb, 1)

            xgt_tile(0, 0, 0)
            xgt_tile(1, 1, 1)
            h_tile(0, 0, 0)
            xgt_tile(2, 0, 2)
            h_tile(1, 1, 1)
            y_tile(0, 0, 0, 0)
            xgt_tile(3, 1, 2)
            h_tile(2, 0, 2)
            y_tile(1, 1, 1, 0)
            with v.Fori(0, 9) as i:
                for d in (2, 3):
                    xgt_tile(2 * i + (d + 2), d % 2, 2)
                    h_tile(2 * i + (d + 1), 1 - d % 2, 2)
                    y_tile(2 * i + d, d % 2, 2, i + 1)
            xgt_tile(22, 0, 2)
            h_tile(21, 1, 2)
            y_tile(20, 0, 2, 10)
            h_tile(22, 0, 2)
            y_tile(21, 1, 2, 10)
            y_tile(22, 0, 2, 11)

            for step in c_steps:
                n, b, i = step
                if n == "Wat":
                    dst = ua_t if i == 0 else da_t[:, 512 * (i - 1):512 * i]
                    w = C if i == 0 else 512
                    nc.vector.tensor_copy(dst[0:RANK, :], filled(v, step)[0:RANK, 0:w]).then_inc(free_of(step), 1)
                elif n == "Wb":
                    src = filled(v, step)
                    tick(nc.vector.tensor_copy(b_up, src[:, 4:4 + NK]))
                    nc.vector.tensor_copy(b_qk, src[:, 0:4]).then_inc(free_of(step), 1)
                    consumed(v, step)
                    nc.vector.tensor_scalar(b_qk[:, 0:2], b_qk[:, 0:2], 0.25, None, ALU.mult).then_inc(bqk_ready, 1)
                elif n == "Wul":
                    c, half = i // 2, i % 2
                    consumed(v, ("Wu", 0, i))
                    dst = w_up[:, c, 512 * half:512 * half + 512]
                    nc.vector.tensor_tensor(dst, filled(v, step), dst, ALU.add).then_inc(free_of(step), 1)
                elif n == "Wdl":
                    consumed(v, ("Wd", 0, i))
                    dst = w_dn[:, 2 * i:2 * i + 2, :].rearrange("p r n -> p (r n)")
                    nc.vector.tensor_tensor(dst, filled(v, step), dst, ALU.add).then_inc(free_of(step), 1)
                elif n == "cL":
                    rows = x_sb[:, NT * b + 2 * i:NT * b + 2 * i + 2, :]
                    v.wait_ge(gathered, 16 * NT * (b + 1))
                    link(nc.vector.tensor_tensor(rows, rows, yrow[:, 2 * i:2 * i + 2, :], ALU.add))
                    stats(b, i, rows)
                    normalise(rows, rows, i, x2_ready, 2 * b + i + 1)
                elif n == "cK":
                    s = i % 2
                    consumed(v, ("cQ", b, i))
                    if i or b:
                        v.wait_ge(cparts_ready, 4 * b + i)
                    link(nc.vector.tensor_tensor(cresid, qf[s], cparts[:, s, 0, :], ALU.subtract))
                    link(nc.vector.tensor_copy(cparts[:, s, 1, :], cresid))
                    nc.vector.tensor_tensor(cparts[:, s, 2, :], cresid, cparts[:, s, 1, :], ALU.subtract)\
                      .then_inc(cparts_ready, 1)
                elif n == "cV":
                    if b == 0 and i == 0:
                        v.wait_ge(s_bias, 48)
                        v.wait_ge(kones, 1)
                    if b >= 2:
                        v.wait_ge(pv_done, head0 * B + headc * (b - 1))
                    src = filled(v, step).rearrange("p (t h d) -> p t h d", t=2, d=HD)
                    for t in range(2):
                        last = nc.vector.tensor_tensor(cv_aug[:, b % 2, 2 * i + t, :, 0:HD], src[:, t, :, :],
                                                       bv_b.rearrange("p (h d) -> p h d", d=HD), ALU.add)
                        if t == 0:
                            tick(last)
                    last.then_inc(free_of(step), 1)
                elif n == "max":
                    qt, h0, nh = MAXES[i]
                    w = P * (qt + 1)
                    if i == 0 and b:
                        v.wait_ge(m_parts, b)
                    nc.vector.tensor_reduce(mneg[:, qt, h0:h0 + nh],
                                            filled(v, step)[:, 0:nh * w].rearrange("p (h n) -> p h n", n=w),
                                            AX.X, ALU.max, negate=True).then_inc(free_of(step), 1)
                elif n == "cM":
                    for i in range(len(MAXES) - UNITS, len(MAXES)):
                        consumed(v, ("max", b, i))
                    link(nc.vector.tensor_copy(mparts[:, :, 0, :], mneg))
                    nc.vector.tensor_tensor(mparts[:, :, 1, :], mneg, mparts[:, :, 0, :], ALU.subtract).then_inc(m_parts, 1)
                elif n == "cF":
                    src = filled(v, step)
                    if i:
                        consumed(v, ("cF", b, i - 1))
                    heads(src, cattn[:, i % 2, :], rden, step)
                elif n == "cP":
                    rows = x_sb[:, NT * b + 2 * i:NT * b + 2 * i + 2, :]
                    src = filled(v, step).rearrange("p (t n) -> p t n", t=2)
                    nc.vector.tensor_tensor(rows, src, rows, ALU.add).then_inc(free_of(step), 1)
                    consumed(v, step)
                    link(nc.vector.tensor_tensor(rows, rows, bo_b.unsqueeze(1).to_broadcast([P, 2, C]), ALU.add))
                    stats(b, i, rows)
                    normalise(rows, rows, i, x3_ready, 2 * b + i + 1)
                elif n == "cD":
                    row = x_sb[:, NT * b + i, :]
                    nc.vector.tensor_tensor(row, filled(v, step)[:, 0:C], row, ALU.add).then_inc(free_of(step), 1)
                    consumed(v, step)
                    link(nc.vector.tensor_tensor(row, row, bd_b, ALU.add))
                elif n == "cO":
                    rows = x_sb[:, NT * b + 2 * i:NT * b + 2 * i + 2, :]
                    stats(b, i, rows)
                    if b and i == 0:
                        v.wait_ge(s_out, 32 * b)
                    normalise(y2[:, 2 * i:2 * i + 2, :], rows, i, y_ready, 2 * b + i + 1)

        @block.gpsimd
        def _(pool):
            pool.wait_ge(slots_ready, 1)
            pool.wait_ge(s_zero, 16)
            pool.wait_ge(s_small, 80)
            for t in range(TT):
                nc.gpsimd.indirect_dma_start(out=id_dram, out_offset=bass.IndirectOffsetOnAxis(ap=slot_i[:, t:t + 1], axis=0),
                                             in_=tok_id[:, t:t + 1], in_offset=None).then_inc(s_scat, 16)
            consumed(pool, ("ID", 0, 0))
            pool.wait_ge(s_xs, 16 * B)
            for j in range(MT):
                if j >= 2:
                    pool.wait_ge(xgt_ps, j - 1)
                nc.gpsimd.indirect_dma_start(out=xg[:, j % 2, :], out_offset=None, in_=xs_dram,
                                             in_offset=bass.IndirectOffsetOnAxis(ap=ids[:, j:j + 1], axis=0))\
                  .then_inc(xg_in[j % 2], 16)
            pool.wait_ge(s_nat, 16 * 10)
            nc.gpsimd.tensor_scalar(n_up, n_up.bitcast(I32), 7.5, None, ALU.subtract).then_inc(poolc, 1)
            pool.wait_ge(poolc, 1)
            up4 = n_up.rearrange("p r (k j) -> p (r k) j", j=BLOCK)
            nc.gpsimd.tensor_tensor(up4, up4, n_ups.rearrange("p r k -> p (r k)").unsqueeze(2)
                                    .to_broadcast([P, NK * C // BLOCK, BLOCK]), ALU.mult).then_inc(deq, 1)
            pool.wait_ge(deq, 1)
            nc.gpsimd.tensor_scalar(n_dn, n_dn.bitcast(I32), 7.5, None, ALU.subtract).then_inc(poolc, 1)
            pool.wait_ge(poolc, 2)
            dn4 = n_dn.rearrange("p r (k j) -> p (r k) j", j=BLOCK)
            nc.gpsimd.tensor_tensor(dn4, dn4, n_dns.rearrange("p r k -> p (r k)").unsqueeze(2)
                                    .to_broadcast([P, 2 * HID // BLOCK, BLOCK]), ALU.mult).then_inc(deq, 1)
            pool.wait_ge(deq, 2)
            pool.wait_ge(y_st[0], 16 * (MT // 2 + 1))
            pool.wait_ge(y_st[1], 16 * (MT // 2))
            pool.wait_ge(y_full, MT)

            def gather(b):
                for t in range(NT):
                    nc.gpsimd.indirect_dma_start(out=yrow[:, t, :], out_offset=None, in_=yg_dram,
                                                 in_offset=bass.IndirectOffsetOnAxis(ap=slot_i[:, NT * b + t:NT * b + t + 1],
                                                                                     axis=0)).then_inc(gathered, 16)

            gather(0)
            ones2 = ck_stack[STACK:STACK + 2].rearrange("p r h n -> p (r h n)")
            nc.gpsimd.memset(cv_aug, 1.0).then_inc(poolc, 1)
            pool.wait_ge(poolc, 3)
            nc.gpsimd.memset(ones2, 1.0).then_inc(kones, 1)
            pool.wait_ge(kones, 1)
            for step in c_steps:
                n, b, i = step
                if n == "cL" and i == 1 and b + 1 < B:
                    pool.wait_ge(x2_ready, 2 * b + 2)
                    gather(b + 1)
                elif n == "cattS":
                    k = head0 * B + headc * b + i
                    kt = i % NT
                    pool.wait_ge(exp_done[0], k + 1)
                    pool.wait_ge(exp_done[1], k + 1)
                    diag = cprobs[:, i % 2, :, P * kt:P * (kt + 1)]
                    nc.gpsimd.affine_select(out=diag, in_=diag, compare_op=ALU.is_ge, fill=0.0, base=0,
                                            pattern=[[0, 4], [1, P]], channel_multiplier=-1).then_inc(masked, 1)


_NAMES = {
    "x": "L0_attn_x", "q_kernel": "L0_attn_q_kernel", "k_kernel": "L0_attn_k_kernel", "v_kernel": "L0_attn_v_kernel",
    "out_kernel": "L0_attn_out_kernel", "router_w": "L0_ffn_router_w", "gate_up_proj": "L0_ffn_gate_up_proj",
    "down_proj": "L0_ffn_down_proj", "shared_gate_w": "L0_ffn_shared_gate_w", "shared_up_w": "L0_ffn_shared_up_w",
    "shared_down_w": "L0_ffn_shared_down_w", "W_qkv": "L1_attn_W_qkv", "b_qkv": "L1_attn_b_qkv",
    "W_out": "L1_attn_W_out", "b_out": "L1_attn_b_out", "w_up_q": "L1_ffn_w_up_q", "w_up_scale": "L1_ffn_w_up_scale",
    "b_up": "L1_ffn_b_up", "w_up_lora_a": "L1_ffn_w_up_lora_a", "w_up_lora_b": "L1_ffn_w_up_lora_b",
    "w_down_q": "L1_ffn_w_down_q", "w_down_scale": "L1_ffn_w_down_scale", "b_down": "L1_ffn_b_down",
    "w_down_lora_a": "L1_ffn_w_down_lora_a", "w_down_lora_b": "L1_ffn_w_down_lora_b",
}


def shape_constants():
    f = np.float32
    fraction = np.arange(0, HD, 2, dtype=f) / f(HD)
    inv_freq = (f(1.0) / np.power(f(10000.0), fraction, dtype=f)).astype(f)
    angle = np.arange(S, dtype=f)[:, None] * inv_freq[None, :]
    sin, cos = np.sin(angle).astype(f), np.cos(angle).astype(f)
    cos = np.concatenate([cos, cos], axis=1)
    sin = np.concatenate([-sin, sin], axis=1)

    def tiled(a):
        return np.ascontiguousarray(a.reshape(NT, P, HD).transpose(1, 0, 2))

    i = np.arange(P)
    return {
        "ident": np.eye(P, dtype=f), "upper": (i[:, None] < i[None, :]).astype(f), "cos": tiled(cos), "sin": tiled(sin),
        "iotae": np.tile(np.arange(E, dtype=f), (P, 1)), "tok_id": np.ascontiguousarray(np.arange(TT * P, dtype=f).reshape(TT, P).T), "iotaj": np.tile(np.arange(24, dtype=f), (P, 1)),
    }


def build(nc, arrays):
    args = {n: nc.dram_tensor(f"in_{n}", a.shape, mybir.dt.from_np(a.dtype), kind="ExternalInput").ap()
            for n, a in arrays.items()}
    out = nc.dram_tensor("out_0", (B, S, C), F32, kind="ExternalOutput").ap()
    post_ln_layers(nc, args, out)


def kernel(**inputs):
    import concourse.bacc as bacc
    from concourse.bass_utils import run_bass_kernel_spmd

    nc = bacc.Bacc("TRN2", target_bir_lowering=False, num_devices=1)
    arrays = {short: np.ascontiguousarray(inputs[name]) for short, name in _NAMES.items()}
    arrays.update(shape_constants())
    build(nc, arrays)
    r = run_bass_kernel_spmd(nc, [{f"in_{n}": a for n, a in arrays.items()}], core_ids=[0])
    return r.results[0]["out_0"]
```
